# Optimizing a Trainium2 kernel written in Bass

```python
import numpy as np
import jax
import jax.numpy as jnp

def _softmax(x, axis=-1):
    return jax.nn.softmax(x, axis=axis)

def _gelu(x):
    return jax.nn.gelu(x, approximate=True)

def _silu(x):
    return jax.nn.silu(x)

def _sigmoid(x):
    return jax.nn.sigmoid(x)

def _layernorm(x, axis=-1, eps=1e-05):
    m = jnp.mean(x, axis=axis, keepdims=True)
    v = jnp.var(x, axis=axis, keepdims=True)
    return (x - m) / jnp.sqrt(v + eps)

def _scatter_add(tgt, idx, src, axis=0):
    return tgt.at[idx].add(src)

def _segment_sum(src, seg, n):
    return jax.ops.segment_sum(src, seg, n)
kernel_name = 'mk_gnn_preln_d4_gnn_r32_81bdca'

def setup_inputs(seed: int=0):
    np.random.seed(seed)
    _w = jnp.asarray

    def _rec_inputs():
        import jax
        import jax.numpy as jnp
        _gk = jax.random.key(seed)
        x = -0.0003713 + 1 * jax.random.normal(jax.random.fold_in(_gk, 1), (3125, 256), jnp.float32)
        src = jax.random.randint(jax.random.fold_in(_gk, 2), (50000,), 0, 3125, jnp.int32)
        dst = jax.random.randint(jax.random.fold_in(_gk, 3), (50000,), 0, 3125, jnp.int32)
        _o = jnp.argsort(dst, stable=True)
        src = src[_o]
        dst = dst[_o]
        edge_attr_128 = 9.41057e-06 + 1 * jax.random.normal(jax.random.fold_in(_gk, 12), (50000, 128), jnp.float32)
        edge_type_8 = jax.random.randint(jax.random.fold_in(_gk, 14), (50000,), 0, 8, jnp.int32)
        edge_weight = jax.random.uniform(jax.random.fold_in(_gk, 15), (50000,), jnp.float32, 0.0, 1)
        node_vec1 = jax.random.uniform(jax.random.fold_in(_gk, 16), (3125, 1), jnp.float32, 0.0, 0.999973)
        node_vec1_n2 = jax.random.uniform(jax.random.fold_in(_gk, 17), (3125, 1), jnp.float32, 0.0, 0.999973)
        return (x, src, dst, edge_attr_128, edge_type_8, edge_weight, node_vec1, node_vec1_n2)
    x, src, dst, edge_attr_128, edge_type_8, edge_weight, node_vec1, node_vec1_n2 = _rec_inputs()

    def _L0_gnn_setup():
        import jax, jax.numpy as jnp
        import numpy as np
        NEG_SLOPE = 0.2
        N_NODES = 50000
        N_EDGES = 25000

        def gat_conv(h, src, dst, W, al, ar, residual):
            N = h.shape[0]
            H, D = al.shape
            feat = (h @ W).reshape(N, H, D)
            el = jnp.sum(feat * al, axis=-1)
            er = jnp.sum(feat * ar, axis=-1)
            e = jax.nn.leaky_relu(el[src] + er[dst], NEG_SLOPE)
            emax = jax.ops.segment_max(e, dst, num_segments=N)
            ex = jnp.exp(e - emax[dst])
            denom = jax.ops.segment_sum(ex, dst, num_segments=N)
            a = ex / denom[dst]
            msg = feat[src] * a[:, :, None]
            rst = jax.ops.segment_sum(msg, dst, num_segments=N)
            if residual:
                rst = rst + h.reshape(N, H, D)
            return jax.nn.elu(rst).reshape(N, H * D)
        key = jax.random.key(seed)
        ks = jax.random.split(key, 9)
        features = jax.random.normal(ks[0], (N_NODES, 256), dtype=jnp.float32)
        src = jax.random.randint(ks[1], (N_EDGES,), 0, N_NODES, dtype=jnp.int32)
        dst = jax.random.randint(ks[2], (N_EDGES,), 0, N_NODES, dtype=jnp.int32)
        s1 = 1.0 / np.sqrt(256.0)
        W1 = jax.random.normal(ks[3], (256, 256), dtype=jnp.float32) * s1
        al1 = jax.random.normal(ks[4], (4, 64), dtype=jnp.float32) * 0.1
        ar1 = jax.random.normal(ks[5], (4, 64), dtype=jnp.float32) * 0.1
        W2 = jax.random.normal(ks[6], (256, 256), dtype=jnp.float32) * s1
        al2 = jax.random.normal(ks[7], (4, 64), dtype=jnp.float32) * 0.1
        ar2 = jax.random.normal(ks[8], (4, 64), dtype=jnp.float32) * 0.1
        return {'features': features, 'src': src, 'dst': dst, 'W1': W1, 'al1': al1, 'ar1': ar1, 'W2': W2, 'al2': al2, 'ar2': ar2}
    _L0_gnn_all = _L0_gnn_setup()
    _L0_gnn_in = {k: v for k, v in _L0_gnn_all.items() if k in ('W1', 'al1', 'ar1', 'W2', 'al2', 'ar2')}
    del _L0_gnn_all

    def _L1_gnn_setup():
        import jax, jax.numpy as jnp
        import numpy as np
        NUM_NODES = 50000
        NUM_EDGES = 50000
        NODE_DIM = 256
        EDGE_DIM = 128
        MAX_IN_DEGREE = 512
        MAX_OUT_DEGREE = 512
        key = jax.random.key(seed)
        ks = jax.random.split(key, 12)
        x = jax.random.normal(ks[0], (NUM_NODES, NODE_DIM), dtype=jnp.float32)
        edge_index = jax.random.randint(ks[1], (2, NUM_EDGES), 0, NUM_NODES, dtype=jnp.int64 if jax.config.read('jax_enable_x64') else jnp.int32)
        edge_attr = jax.random.normal(ks[2], (NUM_EDGES, EDGE_DIM), dtype=jnp.float32)
        voronoi_values = jax.random.uniform(ks[3], (NUM_NODES, 1), dtype=jnp.float32)
        centralities = jax.random.uniform(ks[4], (NUM_NODES, 1), dtype=jnp.float32)
        z_in = jax.random.normal(ks[5], (MAX_IN_DEGREE, NODE_DIM), dtype=jnp.float32)
        z_out = jax.random.normal(ks[6], (MAX_OUT_DEGREE, NODE_DIM), dtype=jnp.float32)
        W_cent = jax.random.normal(ks[7], (1, NODE_DIM), dtype=jnp.float32) * 0.5
        b_cent = jnp.zeros((NODE_DIM,), dtype=jnp.float32)
        W_vor = jax.random.normal(ks[8], (1, NODE_DIM), dtype=jnp.float32) * 0.5
        b_vor = jnp.zeros((NODE_DIM,), dtype=jnp.float32)
        W_sum = jax.random.normal(ks[9], (EDGE_DIM, NODE_DIM), dtype=jnp.float32) * (1.0 / np.sqrt(EDGE_DIM))
        b_sum = jnp.zeros((NODE_DIM,), dtype=jnp.float32)
        return {'x': x, 'edge_index': edge_index, 'edge_attr': edge_attr, 'voronoi_values': voronoi_values, 'centralities': centralities, 'z_in': z_in, 'z_out': z_out, 'W_cent': W_cent, 'b_cent': b_cent, 'W_vor': W_vor, 'b_vor': b_vor, 'W_sum': W_sum, 'b_sum': b_sum}
    _L1_gnn_all = _L1_gnn_setup()
    _L1_gnn_in = {k: v for k, v in _L1_gnn_all.items() if k in ('z_in', 'z_out', 'W_cent', 'b_cent', 'W_vor', 'b_vor', 'W_sum', 'b_sum')}
    del _L1_gnn_all

    def _L2_gnn_setup():
        import jax, jax.numpy as jnp
        import numpy as np
        N_NODES = 50000
        N_EDGES = 25000
        IN_FEAT = 256
        OUT_FEAT = 256
        NUM_RELS = 8
        NUM_BASES = 8
        SUBMAT_IN = IN_FEAT // NUM_BASES
        SUBMAT_OUT = OUT_FEAT // NUM_BASES
        key = jax.random.key(seed)
        k_h, k_w, k_src, k_dst, k_rel, k_norm = jax.random.split(key, 6)
        h = jax.random.normal(k_h, (N_NODES, IN_FEAT), dtype=jnp.float32)
        weight = jax.random.normal(k_w, (NUM_RELS, NUM_BASES * SUBMAT_IN * SUBMAT_OUT), dtype=jnp.float32) * 0.05
        edge_src = jax.random.randint(k_src, (N_EDGES,), 0, N_NODES, dtype=jnp.int32)
        edge_dst = jax.random.randint(k_dst, (N_EDGES,), 0, N_NODES, dtype=jnp.int32)
        edge_rel = jax.random.randint(k_rel, (N_EDGES,), 0, NUM_RELS, dtype=jnp.int32)
        edge_norm = jax.random.uniform(k_norm, (N_EDGES,), dtype=jnp.float32)
        return {'h': h, 'weight': weight, 'edge_src': edge_src, 'edge_dst': edge_dst, 'edge_rel': edge_rel, 'edge_norm': edge_norm}
    _L2_gnn_all = _L2_gnn_setup()
    _L2_gnn_in = {k: v for k, v in _L2_gnn_all.items() if k in ('weight',)}
    del _L2_gnn_all

    def _L3_gnn_setup():
        import jax, jax.numpy as jnp
        import numpy as np
        EPS = 1e-05

        def _bn(x, gamma, beta):
            m = jnp.mean(x, axis=0)
            v = jnp.mean((x - m) ** 2, axis=0)
            return gamma * (x - m) * jax.lax.rsqrt(v + EPS) + beta

        def _hconv(x, src, dst, ew, w1, b1, w2, b2, g, b):
            h = jax.nn.relu(x @ w1 + b1)
            msg = ew[:, None] * h[src]
            agg = jax.ops.segment_sum(msg, dst, num_segments=x.shape[0])
            h = agg @ w2 + b2
            return jax.nn.relu(_bn(h, g, b))
        N, C, E = (50000, 256, 9375)
        key = jax.random.key(seed)
        ks = jax.random.split(key, 16)
        s = 1.0 / np.sqrt(C)
        inp = {'x': jax.random.normal(ks[0], (N, C), dtype=jnp.float32), 'hyperedge_index': jax.random.randint(ks[1], (2, E), 0, N, dtype=jnp.int32), 'hyperedge_weight': jax.random.uniform(ks[2], (E,), dtype=jnp.float32), 'c1_w1': jax.random.normal(ks[3], (C, C), dtype=jnp.float32) * s, 'c1_b1': jnp.zeros((C,), jnp.float32), 'c1_w2': jax.random.normal(ks[4], (C, C), dtype=jnp.float32) * s, 'c1_b2': jnp.zeros((C,), jnp.float32), 'c1_g': jnp.ones((C,), jnp.float32), 'c1_b': jnp.zeros((C,), jnp.float32), 'bn1_g': jnp.ones((C,), jnp.float32), 'bn1_b': jnp.zeros((C,), jnp.float32), 'c2_w1': jax.random.normal(ks[5], (C, C), dtype=jnp.float32) * s, 'c2_b1': jnp.zeros((C,), jnp.float32), 'c2_w2': jax.random.normal(ks[6], (C, C), dtype=jnp.float32) * s, 'c2_b2': jnp.zeros((C,), jnp.float32), 'c2_g': jnp.ones((C,), jnp.float32), 'c2_b': jnp.zeros((C,), jnp.float32), 'bn2_g': jnp.ones((C,), jnp.float32), 'bn2_b': jnp.zeros((C,), jnp.float32)}
        return inp
    _L3_gnn_all = _L3_gnn_setup()
    _L3_gnn_in = {k: v for k, v in _L3_gnn_all.items() if k in ('c1_w1', 'c1_b1', 'c1_w2', 'c1_b2', 'c1_g', 'c1_b', 'bn1_g', 'bn1_b', 'c2_w1', 'c2_b1', 'c2_w2', 'c2_b2', 'c2_g', 'c2_b', 'bn2_g', 'bn2_b')}
    del _L3_gnn_all
    return {'x': x, 'src': src, 'dst': dst, 'edge_attr_128': edge_attr_128, 'edge_type_8': edge_type_8, 'edge_weight': edge_weight, 'node_vec1': node_vec1, 'node_vec1_n2': node_vec1_n2, 'L0_gnn_W1': _L0_gnn_in['W1'], 'L0_gnn_al1': _L0_gnn_in['al1'], 'L0_gnn_ar1': _L0_gnn_in['ar1'], 'L0_gnn_W2': _L0_gnn_in['W2'], 'L0_gnn_al2': _L0_gnn_in['al2'], 'L0_gnn_ar2': _L0_gnn_in['ar2'], 'L1_gnn_z_in': _L1_gnn_in['z_in'], 'L1_gnn_z_out': _L1_gnn_in['z_out'], 'L1_gnn_W_cent': _L1_gnn_in['W_cent'], 'L1_gnn_b_cent': _L1_gnn_in['b_cent'], 'L1_gnn_W_vor': _L1_gnn_in['W_vor'], 'L1_gnn_b_vor': _L1_gnn_in['b_vor'], 'L1_gnn_W_sum': _L1_gnn_in['W_sum'], 'L1_gnn_b_sum': _L1_gnn_in['b_sum'], 'L2_gnn_weight': _L2_gnn_in['weight'], 'L3_gnn_c1_w1': _L3_gnn_in['c1_w1'], 'L3_gnn_c1_b1': _L3_gnn_in['c1_b1'], 'L3_gnn_c1_w2': _L3_gnn_in['c1_w2'], 'L3_gnn_c1_b2': _L3_gnn_in['c1_b2'], 'L3_gnn_c1_g': _L3_gnn_in['c1_g'], 'L3_gnn_c1_b': _L3_gnn_in['c1_b'], 'L3_gnn_bn1_g': _L3_gnn_in['bn1_g'], 'L3_gnn_bn1_b': _L3_gnn_in['bn1_b'], 'L3_gnn_c2_w1': _L3_gnn_in['c2_w1'], 'L3_gnn_c2_b1': _L3_gnn_in['c2_b1'], 'L3_gnn_c2_w2': _L3_gnn_in['c2_w2'], 'L3_gnn_c2_b2': _L3_gnn_in['c2_b2'], 'L3_gnn_c2_g': _L3_gnn_in['c2_g'], 'L3_gnn_c2_b': _L3_gnn_in['c2_b'], 'L3_gnn_bn2_g': _L3_gnn_in['bn2_g'], 'L3_gnn_bn2_b': _L3_gnn_in['bn2_b']}

def reference(x, src, dst, edge_attr_128, edge_type_8, edge_weight, node_vec1, node_vec1_n2, L0_gnn_W1, L0_gnn_al1, L0_gnn_ar1, L0_gnn_W2, L0_gnn_al2, L0_gnn_ar2, L1_gnn_z_in, L1_gnn_z_out, L1_gnn_W_cent, L1_gnn_b_cent, L1_gnn_W_vor, L1_gnn_b_vor, L1_gnn_W_sum, L1_gnn_b_sum, L2_gnn_weight, L3_gnn_c1_w1, L3_gnn_c1_b1, L3_gnn_c1_w2, L3_gnn_c1_b2, L3_gnn_c1_g, L3_gnn_c1_b, L3_gnn_bn1_g, L3_gnn_bn1_b, L3_gnn_c2_w1, L3_gnn_c2_b1, L3_gnn_c2_w2, L3_gnn_c2_b2, L3_gnn_c2_g, L3_gnn_c2_b, L3_gnn_bn2_g, L3_gnn_bn2_b):
    import jax
    import jax.numpy as jnp

    def _L0_gnn_ref(features, src, dst, W1, al1, ar1, W2, al2, ar2):
        import jax, jax.numpy as jnp
        import numpy as np
        NEG_SLOPE = 0.2
        N_NODES = 50000
        N_EDGES = 25000

        def gat_conv(h, src, dst, W, al, ar, residual):
            N = h.shape[0]
            H, D = al.shape
            feat = (h @ W).reshape(N, H, D)
            el = jnp.sum(feat * al, axis=-1)
            er = jnp.sum(feat * ar, axis=-1)
            e = jax.nn.leaky_relu(el[src] + er[dst], NEG_SLOPE)
            emax = jax.ops.segment_max(e, dst, num_segments=N)
            ex = jnp.exp(e - emax[dst])
            denom = jax.ops.segment_sum(ex, dst, num_segments=N)
            a = ex / denom[dst]
            msg = feat[src] * a[:, :, None]
            rst = jax.ops.segment_sum(msg, dst, num_segments=N)
            if residual:
                rst = rst + h.reshape(N, H, D)
            return jax.nn.elu(rst).reshape(N, H * D)
        h = gat_conv(features, src, dst, W1, al1, ar1, residual=False)
        h = gat_conv(h, src, dst, W2, al2, ar2, residual=True)
        return h

    def _L1_gnn_ref(x, edge_index, edge_attr, voronoi_values, centralities, z_in, z_out, W_cent, b_cent, W_vor, b_vor, W_sum, b_sum):
        import jax, jax.numpy as jnp
        import numpy as np
        NUM_NODES = 50000
        NUM_EDGES = 50000
        NODE_DIM = 256
        EDGE_DIM = 128
        MAX_IN_DEGREE = 512
        MAX_OUT_DEGREE = 512
        num_nodes = x.shape[0]
        src = edge_index[0]
        dst = edge_index[1]
        ones = jnp.ones_like(src, dtype=jnp.int32)
        in_deg = jnp.minimum(jax.ops.segment_sum(ones, dst, num_segments=num_nodes), MAX_IN_DEGREE - 1)
        out_deg = jnp.minimum(jax.ops.segment_sum(ones, src, num_segments=num_nodes), MAX_OUT_DEGREE - 1)
        edge_proj = edge_attr @ W_sum + b_sum
        sum3d = jax.ops.segment_sum(edge_proj, src, num_segments=num_nodes)
        cent_term = jax.nn.sigmoid(centralities @ W_cent + b_cent)
        vor_term = jax.nn.sigmoid(voronoi_values @ W_vor + b_vor)
        return x + z_in[in_deg] + z_out[out_deg] + cent_term + vor_term + sum3d

    def _L2_gnn_ref(h, weight, edge_src, edge_dst, edge_rel, edge_norm):
        import jax, jax.numpy as jnp
        import numpy as np
        N_NODES = 50000
        N_EDGES = 25000
        IN_FEAT = 256
        OUT_FEAT = 256
        NUM_RELS = 8
        NUM_BASES = 8
        SUBMAT_IN = IN_FEAT // NUM_BASES
        SUBMAT_OUT = OUT_FEAT // NUM_BASES
        'RGCNBlockLayer forward (self_loop=False, bias=None, activation=None).\n\n            Per relation r: agg_r[v] = sum_{(u->v) in rel r} norm_e * h[u]\n            then block-diagonal matmul out_r = blockmm(agg_r, W_r); output = sum_r out_r.\n            '
        N, in_feat = h.shape
        R = weight.shape[0]
        msg = h[edge_src] * edge_norm[:, None]
        seg = edge_rel * N + edge_dst
        agg = jax.ops.segment_sum(msg, seg, num_segments=R * N)
        agg = agg.reshape(R, N, NUM_BASES, SUBMAT_IN)
        W = weight.reshape(R, NUM_BASES, SUBMAT_IN, SUBMAT_OUT)
        out = jnp.einsum('rnbi,rbio->nbo', agg, W)
        return out.reshape(N, NUM_BASES * SUBMAT_OUT)

    def _L3_gnn_ref(x, hyperedge_index, hyperedge_weight, c1_w1, c1_b1, c1_w2, c1_b2, c1_g, c1_b, bn1_g, bn1_b, c2_w1, c2_b1, c2_w2, c2_b2, c2_g, c2_b, bn2_g, bn2_b):
        import jax, jax.numpy as jnp
        import numpy as np
        EPS = 1e-05

        def _bn(x, gamma, beta):
            m = jnp.mean(x, axis=0)
            v = jnp.mean((x - m) ** 2, axis=0)
            return gamma * (x - m) * jax.lax.rsqrt(v + EPS) + beta

        def _hconv(x, src, dst, ew, w1, b1, w2, b2, g, b):
            h = jax.nn.relu(x @ w1 + b1)
            msg = ew[:, None] * h[src]
            agg = jax.ops.segment_sum(msg, dst, num_segments=x.shape[0])
            h = agg @ w2 + b2
            return jax.nn.relu(_bn(h, g, b))
        src, dst = (hyperedge_index[0], hyperedge_index[1])
        residual = x
        h = _hconv(x, src, dst, hyperedge_weight, c1_w1, c1_b1, c1_w2, c1_b2, c1_g, c1_b)
        h = jax.nn.relu(_bn(h, bn1_g, bn1_b))
        h = _hconv(h, src, dst, hyperedge_weight, c2_w1, c2_b1, c2_w2, c2_b2, c2_g, c2_b)
        h = _bn(h, bn2_g, bn2_b)
        return jax.nn.relu(h + residual)
    edge_index = jnp.stack([src, dst])
    h = jnp.maximum(_layernorm(x, axis=-1), 0.0)
    x = x + _L0_gnn_ref(h, src, dst, L0_gnn_W1, L0_gnn_al1, L0_gnn_ar1, L0_gnn_W2, L0_gnn_al2, L0_gnn_ar2)
    h = jnp.maximum(_layernorm(x, axis=-1), 0.0)
    x = x + _L1_gnn_ref(h, edge_index, edge_attr_128, node_vec1, node_vec1_n2, L1_gnn_z_in, L1_gnn_z_out, L1_gnn_W_cent, L1_gnn_b_cent, L1_gnn_W_vor, L1_gnn_b_vor, L1_gnn_W_sum, L1_gnn_b_sum)
    h = jnp.maximum(_layernorm(x, axis=-1), 0.0)
    x = x + _L2_gnn_ref(h, L2_gnn_weight, src, dst, edge_type_8, edge_weight)
    h = jnp.maximum(_layernorm(x, axis=-1), 0.0)
    x = x + _L3_gnn_ref(h, edge_index, edge_weight, L3_gnn_c1_w1, L3_gnn_c1_b1, L3_gnn_c1_w2, L3_gnn_c1_b2, L3_gnn_c1_g, L3_gnn_c1_b, L3_gnn_bn1_g, L3_gnn_bn1_b, L3_gnn_c2_w1, L3_gnn_c2_b1, L3_gnn_c2_w2, L3_gnn_c2_b2, L3_gnn_c2_g, L3_gnn_c2_b, L3_gnn_bn2_g, L3_gnn_bn2_b)
    return x

_drawn_inputs = setup_inputs


def setup_inputs(seed=0):
    import zlib

    import numpy as np

    out = dict(_drawn_inputs(seed))
    spreads = {'L1_gnn_b_cent': (0.0, 2.0),
     'L1_gnn_b_vor': (0.0, 2.0),
     'L1_gnn_b_sum': (0.0, 0.1),
     'L3_gnn_c1_b1': (0.0, 0.1),
     'L3_gnn_c1_b2': (0.0, 2.0),
     'L3_gnn_c1_g': (1.0, 0.6),
     'L3_gnn_c1_b': (0.0, 0.8),
     'L3_gnn_bn1_g': (1.0, 0.2),
     'L3_gnn_bn1_b': (0.0, 0.53),
     'L3_gnn_c2_b1': (0.0, 0.333),
     'L3_gnn_c2_b2': (0.0, 2.0),
     'L3_gnn_c2_g': (1.0, 0.6),
     'L3_gnn_c2_b': (0.0, 0.8),
     'L3_gnn_bn2_g': (1.0, 0.2),
     'L3_gnn_bn2_b': (0.0, 0.653)}
    factors = {'node_vec1': 8.0,
     'node_vec1_n2': 8.0,
     'L0_gnn_al1': 4.2,
     'L0_gnn_ar1': 8.0,
     'L0_gnn_al2': 25.192,
     'L0_gnn_ar2': 55.928,
     'L1_gnn_W_cent': 3.991,
     'L1_gnn_W_vor': 4.258}
    for name, (base, spread) in spreads.items():
        noise = np.random.default_rng([zlib.crc32(name.encode()), seed]).standard_normal(out[name].shape)
        drawn = base * np.exp(spread * noise) if base else spread * noise
        out[name] = jnp.asarray(drawn.astype(out[name].dtype))
    for name, factor in factors.items():
        out[name] = (out[name] * factor).astype(out[name].dtype)
    return out
```

```python
from contextlib import ExitStack

import concourse.bass as bass
from concourse import mybir

ALU = mybir.AluOpType
ACT = mybir.ActivationFunctionType
AX = mybir.AxisListType
F32 = mybir.dt.float32
I32 = mybir.dt.int32
BF16 = mybir.dt.bfloat16

P = 128
N = 3125
E = 50000
D = 256
HEADS = 4
HD = D // HEADS
KD = D // P
AD = 128
RELS = 8
NT = -(-N // P)
NP = NT * P
EC = -(-E // P) + 1
EP = EC * P
S = EC + NT - 1
SLOTS = 16
HALF = 8
PAD_NODE = NP - 1
BIG = 1.0e30
LN_EPS = 1e-5
BN_EPS = 1e-5
RW = 264
W_GAT = D + HEADS + 1
AW = 130
ACCW = 264
assert EC % 28 == 0 and S % 32 == 0 and S <= 4 * P


class Signal:

    def __init__(self, sem):
        self.sem = sem
        self.at = 0


def gnn_program(nc, t, out):
    life = ExitStack()

    def sb(name, shape, dt=F32, scope=None):
        return (scope or life).enter_context(nc.sbuf_tensor(name, shape, dt))

    def psum(name, shape, dt=F32, scope=None):
        return (scope or life).enter_context(nc.psum_tensor(name, shape, dt))

    phase_sems = []

    def sem(name):
        phase_sems.append(nc.alloc_semaphore(name))
        return phase_sems[-1]

    def lasting_sem(name):
        return life.enter_context(nc.semaphore(name))

    def end_phase():
        nc.clear_and_free_semaphores(phase_sems)
        phase_sems.clear()
        nc.all_engine_barrier()

    def dram(name, shape, dt=F32):
        return nc.dram_tensor(name, shape, dt, kind="Internal").ap()

    feat_d = dram("feat_d", [NP, D])
    rel_d = dram("rel_d", [NP * RELS, D])
    weight_d = dram("weight_d", [EC, P * HEADS])
    lo_d = dram("lo_d", [2, EC, P], BF16)
    attr_d = dram("attr_d", [S * P, AW])

    X = sb("X", [P, NT, D])
    HB = sb("HB", [P, NT, D])
    ident = sb("ident", [P, P])
    before = sb("before", [P, P])
    upto = sb("upto", [P, P])
    ones = sb("ones", [P, P])
    lane = sb("lane", [P, P])
    part = sb("part", [P, 1])
    tile_no = sb("tile_no", [P, NT])
    step_no = sb("step_no", [P, S])
    srcS = sb("srcS", [P, S], I32)
    relS = sb("relS", [P, S], I32)
    dlocS = sb("dlocS", [P, S])
    wS = sb("wS", [P, S])
    exS = sb("exS", [P, S, HEADS])
    tileS = sb("tileS", [P, S], I32)
    tileA = sb("tileA", [P, S], I32)
    src_lo = sb("src_lo", [P, EC])
    attr_pos = sb("attr_pos", [P, EC], I32)
    in_deg = sb("in_deg", [P, NT])
    stats = sb("stats", [P, NT, 8])
    mv = sb("mv", [P, NT, 2])
    rstd = sb("rstd", [P, NT])
    shift = sb("shift", [P, NT])

    ring_ready = [Signal(lasting_sem(f"ring_ready{k}")) for k in range(SLOTS)]
    rows_ready = [Signal(lasting_sem(f"rows_ready{h}")) for h in range(4)]
    index_ready = Signal(lasting_sem("index_ready"))
    operands_ready = Signal(lasting_sem("operands_ready"))
    step_done = Signal(lasting_sem("step_done"))
    added = Signal(lasting_sem("added"))

    def layer_norm(tag):
        s_mv, s_sqrt, s_sc = sem(tag + "_mv"), sem(tag + "_sqrt"), sem(tag + "_sc")
        with nc.Block() as block:
            @block.vector
            def _(dve):
                with dve.Fori(0, NT) as n:
                    dve.bn_stats(stats[:, n, 0:6], X[:, n, :])
                dve.drain()
                for n in range(NT):
                    dve.bn_aggr(mv[:, n, :], stats[:, n, 0:6])
                dve.drain()
                dve.tensor_scalar(rstd[:, :], mv[:, :, 1], LN_EPS, None, ALU.add).then_inc(s_mv, 1)
                dve.wait_ge(s_sqrt, 1)
                dve.reciprocal(rstd[:, :], rstd[:, :])
                dve.drain()
                dve.scalar_tensor_tensor(out=shift[:, :], in0=mv[:, :, 0], scalar=-1.0, in1=rstd[:, :],
                                         op0=ALU.mult, op1=ALU.mult).then_inc(s_sc, 1)

            @block.scalar
            def _(act):
                act.wait_ge(s_mv, 1)
                act.activation(rstd[:, :], rstd[:, :], ACT.Sqrt).then_inc(s_sqrt, 1)
                act.wait_ge(s_sc, 1)
                with act.Fori(0, NT) as n:
                    act.activation(HB[:, n, :], X[:, n, :], ACT.Relu, bias=shift[:, bass.ds(n, 1)],
                                   scale=rstd[:, bass.ds(n, 1)])

    def to_feature_major(tag, src, dst, halves):
        s_t, s_c = sem(tag + "_turned"), sem(tag + "_copied")
        with ExitStack() as scope:
            pt = [psum(f"{tag}_pt{k}", [P, 512], scope=scope) for k in range(5)]
            with nc.Block() as block:
                @block.tensor
                def _(pe):
                    pe.sem_inc(s_c, 5)
                    for i in range(5):
                        for k in range(5):
                            pe.wait_ge(s_c, 5 * i + (k + 1))
                            for c in range(halves):
                                last = pe.transpose(pt[k][:, c * P:(c + 1) * P],
                                                    src[:, 5 * i + k, c * P:(c + 1) * P], ident[:, :])
                            last.then_inc(s_t, 1)

                @block.scalar
                def _(act):
                    with act.Fori(0, 5) as i:
                        for k in range(5):
                            act.wait_ge(s_t, 5 * i + (k + 1))
                            act.activation(dst[:, :, bass.ds((5 * i + k) * P, P)],
                                           pt[k][:, 0:halves * P].rearrange("p (c m) -> p c m", c=halves),
                                           ACT.Copy).then_inc(s_c, 1)

    def aggregate(tag, table, index, acc, kind, odd=None):
        width = {"gat": W_GAT, "edge": D, "attr": AW - 1}[kind]
        RING, NHOT, NPS, LAG = (32, 16, 8, HALF) if kind == "attr" else (SLOTS, 4, 4, 2)
        TURNS = S // RING
        ready = [r.at for r in ring_ready]
        idx0, ops0, done0, add0 = index_ready.at, operands_ready.at, step_done.at, added.at
        tiles = tileA if kind == "attr" else tileS
        with ExitStack() as scope:
            ring = sb(tag + "_ring", [P, RING, AW if kind == "attr" else RW], scope=scope)
            hot = sb(tag + "_hot", [P, NHOT, P], scope=scope)
            islot = sb(tag + "_islot", [P, RING], I32, scope=scope)
            ps = [psum(f"{tag}_ps{k}", [P, 512], scope=scope) for k in range(NPS)]
            s_init = sem(tag + "_init")
            block = scope.enter_context(nc.Block())

            if kind == "attr":
                @block.sync
                def _(sp):
                    rows = attr_d.rearrange("(p s) f -> p s f", p=P)
                    with sp.Fori(0, TURNS) as i:
                        for h in range(RING // HALF):
                            sp.wait_ge(step_done.sem, RING * i + (done0 + HALF * (h + 1)))
                            sp.dma_start(ring[:, h * HALF:(h + 1) * HALF, 0:AW],
                                         rows[:, bass.ds(RING * i + h * HALF, HALF), :])\
                              .then_inc(rows_ready[h].sem, 16)
            else:
                @block.scalar
                def _(act):
                    with act.Fori(0, TURNS) as i:
                        for h in range(2):
                            s0 = RING * i + h * HALF
                            act.wait_ge(step_done.sem, RING * i + (done0 + HALF * (h + 1)))
                            if kind == "gat":
                                act.copy(ring[:, h * HALF:(h + 1) * HALF, D:D + HEADS],
                                         exS[:, bass.ds(s0, HALF), :])
                            act.copy(islot[:, h * HALF:(h + 1) * HALF], index[:, bass.ds(s0, HALF)])\
                               .then_inc(index_ready.sem, 1)

                @block.gpsimd
                def _(pool):
                    if kind == "gat":
                        pool.memset(ring[:, :, D + HEADS:W_GAT], 1.0)
                    pool.drain()
                    pool.sem_inc(s_init, 1)
                    with pool.Fori(0, TURNS) as i:
                        for h in range(2):
                            pool.wait_ge(index_ready.sem, 2 * i + (idx0 + h + 1))
                            pool.sem_inc(s_init, 1)
                            for k in range(h * HALF, (h + 1) * HALF):
                                pool.indirect_dma_start(
                                    out=ring[:, k, 0:D], out_offset=None, in_=table,
                                    in_offset=bass.IndirectOffsetOnAxis(ap=islot[:, k:k + 1], axis=0),
                                ).then_inc(ring_ready[k].sem, 16)

            @block.vector
            def _(dve):
                regs = [dve.alloc_register(f"{tag}_tile{k}") for k in range(RING)]

                def add_step(s, node_tile, k):
                    if kind != "attr":
                        dve.wait_ge(step_done.sem, s + (done0 + RING + 1))
                        dve.wait_ge(added.sem, s + (add0 + NPS))
                    elif k % 2 == 0:
                        dve.wait_ge(step_done.sem, s + (done0 + RING + 2))
                        dve.wait_ge(added.sem, s + (add0 + NPS))
                    into = acc if k % 2 == 0 or kind != "attr" else odd
                    dve.tensor_tensor(into[:, node_tile, 0:width], into[:, node_tile, 0:width],
                                      ps[k % NPS][:, 0:width], ALU.add).then_inc(added.sem, 1)

                def turn(i, first=False):
                    base = RING * i
                    skip = LAG if first else 0
                    dve.reg_load(regs[skip:], tiles[0:1, bass.ds(base + (skip - LAG), RING - skip)])
                    late = [None] * skip + [dve.snap(r, min_val=0, max_val=NT - 1) for r in regs[skip:]]
                    for k in range(RING):
                        s = base + k
                        if kind != "attr":
                            dve.wait_ge(step_done.sem, s + (done0 + RING - NHOT + 1))
                        if kind == "attr":
                            if k % HALF == 0:
                                dve.wait_ge(step_done.sem, s + (done0 + RING - NHOT + HALF))
                                dve.wait_ge(rows_ready[k // HALF].sem,
                                            16 * i + (rows_ready[k // HALF].at + 16))
                                dve.tensor_tensor(
                                    hot[:, k % NHOT:k % NHOT + HALF, :],
                                    lane[:, :].unsqueeze(1).to_broadcast([P, HALF, P]),
                                    ring[:, k:k + HALF, AW - 1].unsqueeze(2).to_broadcast([P, HALF, P]),
                                    ALU.is_equal).then_inc(operands_ready.sem, HALF)
                        elif kind == "gat":
                            dve.tensor_scalar(hot[:, k % NHOT, :], lane[:, :], dlocS[:, bass.ds(s, 1)],
                                              None, ALU.is_equal)
                            dve.wait_ge(ring_ready[k].sem, 16 * i + (ready[k] + 16))
                            rows = ring[:, k, 0:D].rearrange("p (h d) -> p h d", h=HEADS)
                            dve.tensor_tensor(rows, rows,
                                              ring[:, k, D:D + HEADS].unsqueeze(2)
                                              .to_broadcast([P, HEADS, HD]), ALU.mult)\
                               .then_inc(operands_ready.sem, 1)
                        else:
                            dve.tensor_scalar(hot[:, k % NHOT, :], lane[:, :], dlocS[:, bass.ds(s, 1)],
                                              wS[:, bass.ds(s, 1)], ALU.is_equal, ALU.mult)\
                               .then_inc(operands_ready.sem, 1)
                        if k >= skip:
                            add_step(s - LAG, late[k], (k - LAG) % RING)

                dve.memset(acc[:, :, :], 0.0)
                if kind == "attr":
                    dve.memset(odd[:, :, :], 0.0)
                dve.drain()
                turn(0, first=True)
                with dve.Fori(1, TURNS) as i:
                    turn(i)
                dve.reg_load(regs[0:LAG], tiles[0:1, S - LAG:S])
                for k in range(LAG):
                    add_step(S - LAG + k, dve.snap(regs[k], min_val=0, max_val=NT - 1), (S - LAG + k) % NPS)
                if kind == "attr":
                    dve.drain()
                    dve.tensor_tensor(acc[:, :, 0:width], acc[:, :, 0:width], odd[:, :, 0:width], ALU.add)

            @block.tensor
            def _(pe):
                pe.sem_inc(step_done.sem, RING)
                pe.sem_inc(added.sem, NPS)
                with pe.Fori(0, TURNS) as i:
                    for k in range(RING):
                        s = RING * i + k
                        if kind != "attr":
                            pe.wait_ge(operands_ready.sem, s + (ops0 + 1))
                            pe.wait_ge(added.sem, s + (add0 + 1))
                        if kind == "edge":
                            pe.wait_ge(ring_ready[k].sem, 16 * i + (ready[k] + 16))
                        if kind == "attr" and k % HALF == 0:
                            pe.wait_ge(operands_ready.sem, s + (ops0 + HALF))
                        if kind == "attr" and k % 2 == 0:
                            pe.wait_ge(added.sem, s + (add0 + 2))
                        pe.matmul(ps[k % NPS][:, 0:width], hot[:, k % NHOT, :], ring[:, k, 0:width],
                                  start=True, stop=True).then_inc(step_done.sem, 1)
        for r in (rows_ready if kind == "attr" else ring_ready):
            r.at += 16 * TURNS
        index_ready.at += 0 if kind == "attr" else 2 * TURNS
        operands_ready.at += S
        step_done.at += S + RING
        added.at += S + NPS

    edges = ExitStack()
    mask = sb("mask", [P, EC, 2 * NT], BF16, edges)
    reset_b = sb("reset_b", [P, EC], scope=edges)
    reset_e = sb("reset_e", [P, EC], scope=edges)
    s_load, s_dst, s_pool = sem("load"), sem("load_dst"), sem("constants")
    cleared = lasting_sem("cleared")
    zeros = sb("zeros", [P, 16 * AW], scope=edges)
    s_int, s_lot, s_loc, s_low = sem("ints"), sem("lo_turned"), sem("lo_copied"), sem("lo_written")
    with ExitStack() as scope:
        src_i = sb("src_i", [P, EC], I32, scope)
        dst_i = sb("dst_i", [P, 3, EC], I32, scope)
        tmp_i = sb("tmp_i", [P, 2, EC], I32, scope)
        hi_f = sb("hi_f", [P, 2, EC], scope=scope)
        dst_lo = sb("dst_lo", [P, EC], scope=scope)
        dst_f = sb("dst_f", [P, 3, EC], scope=scope)
        consts_i = sb("consts_i", [P, S], I32, scope)
        consts_j = sb("consts_j", [P, P], I32, scope)
        consts_k = sb("consts_k", [P, 1], I32, scope)
        loT = sb("loT", [P, 8, P], BF16, scope)
        pl = [psum(f"pl{k}", [P, 512], scope=scope) for k in range(2)]
        QC = EC // 4
        s_pc = sem("constants_i")
        with nc.Block() as block:
            @block.sync
            def _(sp):
                sp.dma_start(src_i[:, :], t["src"].rearrange("(p j) -> p j", p=P)).then_inc(s_dst, 16)
                for q in range(3):
                    sp.dma_start(dst_i[:, q, :], t["dst_ext"][q:q + EP].rearrange("(p j) -> p j", p=P))\
                      .then_inc(s_dst, 16)
                sp.dma_start(X[:, :, :], t["x"].rearrange("(n p) f -> p n f", p=P)).then_inc(s_load, 16)
                for q in range(2):
                    for c in range(4):
                        sp.wait_ge(s_loc, 4 * q + c + 1)
                        sp.dma_start(lo_d[q, c * QC:(c + 1) * QC, :], loT[0:QC, 4 * q + c, :])\
                          .then_inc(s_low, 16)
                sp.wait_ge(s_load, 16)
                sp.wait_ge(s_low, 16 * 8)

            @block.gpsimd
            def _(pool):
                pool.iota(consts_i[:, :], pattern=[[1, S]], base=0, channel_multiplier=0)
                pool.iota(consts_j[:, :], pattern=[[1, P]], base=0, channel_multiplier=0)
                pool.iota(consts_k[:, :], pattern=[[0, 1]], base=0, channel_multiplier=1)\
                    .then_inc(s_pc, 1)
                pool.memset(ones[:, :], 1.0)
                pool.memset(ident[:, :], 0.0)
                pool.memset(before[:, :], 1.0)
                pool.memset(upto[:, :], 1.0)
                pool.drain()
                pool.affine_select(out=ident[:, :], in_=ident[:, :], compare_op=ALU.not_equal, fill=1.0,
                                   base=0, pattern=[[-1, P]], channel_multiplier=1)
                pool.affine_select(out=before[:, :], in_=before[:, :], compare_op=ALU.is_gt, fill=0.0,
                                   base=0, pattern=[[1, P]], channel_multiplier=-1)
                pool.affine_select(out=upto[:, :], in_=upto[:, :], compare_op=ALU.is_ge, fill=0.0,
                                   base=0, pattern=[[1, P]], channel_multiplier=-1).then_inc(s_pool, 1)

            @block.vector
            def _(dve):
                dve.wait_ge(s_pc, 1)
                dve.tensor_copy(lane[:, :], consts_j[:, :])
                dve.tensor_copy(part[:, :], consts_k[:, :])
                dve.tensor_copy(tile_no[:, :], consts_i[:, 0:NT])
                dve.tensor_copy(step_no[:, :], consts_i[:, :])
                dve.wait_ge(s_dst, 16 * 4)
                for q, ids in enumerate((src_i[:, :], dst_i[:, 1, :])):
                    dve.tensor_scalar(tmp_i[:, q, :], ids, P - 1, None, ALU.bitwise_and)
                dve.drain()
                dve.tensor_copy(src_lo[:, :], tmp_i[:, 0, :])
                dve.tensor_copy(dst_lo[:, :], tmp_i[:, 1, :]).then_inc(s_int, 1)
                dve.drain()
                for q, ids in enumerate((src_i[:, :], dst_i[:, 1, :])):
                    dve.tensor_scalar(tmp_i[:, q, :], ids, 7, None, ALU.logical_shift_right)
                dve.drain()
                dve.tensor_copy(hi_f[:, :, :], tmp_i[:, :, :])
                dve.tensor_copy(dst_f[:, :, :], dst_i[:, :, :])
                dve.drain()
                for q in range(2):
                    dve.tensor_tensor(mask[:, :, q * NT:(q + 1) * NT],
                                      tile_no[:, :].unsqueeze(1).to_broadcast([P, EC, NT]),
                                      hi_f[:, q, :].unsqueeze(2).to_broadcast([P, EC, NT]), ALU.is_equal)
                for reset, other in ((reset_b, 0), (reset_e, 2)):
                    dve.tensor_tensor(reset[:, :], dst_f[:, 1, :], dst_f[:, other, :], ALU.not_equal)
                dve.drain()
                for reset in (reset_b, reset_e):
                    dve.tensor_scalar(reset[:, :], reset[:, :], -BIG, None, ALU.mult)
                for n in range(8):
                    dve.wait_ge(s_lot, n + 1)
                    dve.tensor_copy(loT[0:QC, n, :], pl[n % 2][0:QC, 0:P]).then_inc(s_loc, 1)

            @block.tensor
            def _(pe):
                pe.wait_ge(s_pool, 1)
                pe.wait_ge(s_int, 1)
                for n in range(8):
                    lo = (src_lo, dst_lo)[n // 4]
                    if n >= 2:
                        pe.wait_ge(s_loc, n - 1)
                    pe.transpose(pl[n % 2][0:QC, 0:P], lo[:, (n % 4) * QC:(n % 4 + 1) * QC], ident[:, :])\
                      .then_inc(s_lot, 1)

    s_sl, s_gr, s_cmp, s_nrow, s_tcol, s_idx = (sem("steps_load"), sem("steps_rows"), sem("steps_cmp"),
                                                sem("steps_tile"), sem("steps_edge_tile"), sem("steps_index"))
    s_sp = sem("steps_spread")
    s_fl, s_tr, s_cp = sem("steps_float"), sem("steps_turned"), sem("steps_copied")
    with ExitStack() as scope:
        last_i = sb("last_i", [32, EC], I32, scope)
        last_f = sb("last_f", [32, EC], scope=scope)
        bound = sb("bound", [32, 2], scope=scope)
        passed = sb("passed", [32, S], scope=scope)
        tile_f = sb("tile_f", [P, S], scope=scope)
        edge_tile = sb("edge_tile", [P, 4], I32, scope)
        rows_i = sb("rows_i", [P, 3, 4, P], I32, scope)
        rows_f = sb("rows_f", [P, 4, 4, P], scope=scope)
        stepT = sb("stepT", [P, 4, S], scope=scope)
        pr = psum("pr", [P, 512], scope=scope)
        pc = psum("pc", [P, 512], scope=scope)
        pt = [psum(f"pst{k}", [P, 512], scope=scope) for k in range(4)]
        NG = [min(P, S - P * g) for g in range(4)]
        tables = [t["src"], t["dst"], t["type"], t["weight"]]
        with nc.Block() as block:
            @block.sync
            def _(sp):
                sp.dma_start(last_i[0:1, :], t["dst"].rearrange("(e p) -> e p", p=P)[:, P - 1].unsqueeze(0),
                             allow_slow_non_contiguous=True).then_inc(s_sl, 16)

            @block.vector
            def _(dve):
                dve.wait_ge(s_sl, 16)
                dve.tensor_copy(last_f[0:1, :], last_i[0:1, :]).then_inc(s_sp, 1)
                dve.tensor_scalar(bound[0:NT, 0:1], part[0:NT, :], float(P), float(P), ALU.mult, ALU.add)
                dve.drain()
                dve.wait_ge(s_sp, 2)
                dve.tensor_scalar(last_f[0:NT, :], pc[0:NT, 0:EC], bound[0:NT, 0:1], None, ALU.is_lt)
                dve.drain()
                dve.reduce_sum(bound[0:NT, 1:2], last_f[0:NT, :], AX.X)
                dve.drain()
                dve.tensor_tensor(bound[0:NT, 0:1], bound[0:NT, 1:2], part[0:NT, :], ALU.add)
                dve.drain()
                dve.tensor_scalar(passed[0:NT, :], step_no[0:NT, :], bound[0:NT, 0:1], None, ALU.is_gt)\
                   .then_inc(s_cmp, 1)
                dve.wait_ge(s_nrow, 1)
                dve.tensor_copy(tile_f[:, :], pr[:, 0:S])
                dve.tensor_copy(tileS[:, :], pr[:, 0:S])
                dve.drain()
                for g in range(4):
                    dve.tensor_scalar(edge_tile[0:NG[g], g:g + 1], pc[0:NG[g], g:g + 1], -1.0, float(P * g),
                                      ALU.mult, ALU.add)
                dve.drain()
                for g in range(4):
                    last = dve.tensor_scalar(edge_tile[0:NG[g], g:g + 1], edge_tile[0:NG[g], g:g + 1],
                                             part[0:NG[g], :], None, ALU.add)
                last.then_inc(s_idx, 1)
                dve.wait_ge(s_gr, 16 * 16)
                for q in range(3):
                    for g in range(4):
                        dve.tensor_copy(rows_f[0:NG[g], q, g, :], rows_i[0:NG[g], q, g, :])
                dve.drain()
                dve.sem_inc(s_fl, 1)
                for n in range(16):
                    q, g = n // 4, n % 4
                    dve.wait_ge(s_tr, n + 1)
                    dve.tensor_copy(stepT[:, q, g * P:g * P + NG[g]], pt[n % 4][:, 0:NG[g]]).then_inc(s_cp, 1)
                dve.drain()
                dve.tensor_copy(srcS[:, :], stepT[:, 0, :])
                dve.scalar_tensor_tensor(out=dlocS[:, :], in0=tile_f[:, :], scalar=-float(P),
                                         in1=stepT[:, 1, :], op0=ALU.mult, op1=ALU.add)
                dve.scalar_tensor_tensor(out=relS[:, :], in0=stepT[:, 0, :], scalar=float(RELS),
                                         in1=stepT[:, 2, :], op0=ALU.mult, op1=ALU.add)
                dve.tensor_copy(wS[:, :], stepT[:, 3, :])

            @block.tensor
            def _(pe):
                pe.wait_ge(s_sp, 1)
                pe.matmul(pc[0:NT, 0:EC], ones[0:1, 0:NT], last_f[0:1, :], start=True, stop=True)\
                  .then_inc(s_sp, 1)
                pe.wait_ge(s_cmp, 1)
                pe.matmul(pr[:, 0:S], ones[0:NT - 1, :], passed[0:NT - 1, :], start=True, stop=True)
                for g in range(4):
                    last = pe.matmul(pc[0:NG[g], g:g + 1], passed[0:NT - 1, g * P:g * P + NG[g]],
                                     ones[0:NT - 1, 0:1], start=True, stop=True)
                last.then_inc(s_nrow, 1)
                pe.wait_ge(s_fl, 1)
                for n in range(16):
                    q, g = n // 4, n % 4
                    if n >= 4:
                        pe.wait_ge(s_cp, n - 3)
                    pe.transpose(pt[n % 4][:, 0:NG[g]], rows_f[0:NG[g], q, g, :], ident[0:NG[g], 0:NG[g]])\
                      .then_inc(s_tr, 1)

            @block.gpsimd
            def _(pool):
                pool.wait_ge(s_idx, 1)
                for q in range(4):
                    for g in range(4):
                        dst = rows_i[0:NG[g], q, g, :] if q < 3 else rows_f[0:NG[g], 3, g, :]
                        pool.indirect_dma_start(
                            out=dst, out_offset=None, in_=tables[q].rearrange("(e p) -> e p", p=P),
                            in_offset=bass.IndirectOffsetOnAxis(ap=edge_tile[0:NG[g], g:g + 1], axis=0),
                        ).then_inc(s_gr, 16)

    s_tot, s_pre, s_nst, s_end, s_bst, s_arow = (sem("attr_totals"), sem("attr_prefix"), sem("attr_steps"),
                                                 sem("attr_ends"), sem("attr_cmp"), sem("attr_tiles"))
    with ExitStack() as scope:
        total = sb("total", [P, NT], scope=scope)
        steps_i = sb("steps_i", [P, NT], I32, scope)
        steps_f = sb("steps_f", [P, NT], scope=scope)
        ends = sb("ends", [P, NT], scope=scope)
        offset = sb("offset", [P, NT], scope=scope)
        col_i = sb("col_i", [32, 1], I32, scope)
        col_f = sb("col_f", [32, 2], scope=scope)
        passed = sb("passed_a", [32, S], scope=scope)
        rank = sb("rank", [P, EC], scope=scope)
        pos = sb("pos", [P, EC], scope=scope)
        one_row = sb("one_row", [P, EC], scope=scope)
        place_i = sb("place_i", [P, 2, EC], I32, scope)
        pp = psum("pp", [P, 512], scope=scope)
        pq = psum("pq", [P, 512], scope=scope)
        px = psum("px", [P, 512], scope=scope)
        s_zero = sem("zeros_ready")
        with nc.Block() as block:
            @block.gpsimd
            def _(pool):
                pool.memset(zeros[:, :], 0.0).then_inc(s_zero, 1)

            @block.sync
            def _(sp):
                sp.wait_ge(s_zero, 1)
                grouped = attr_d.rearrange("(p r) f -> p (r f)", p=P)
                for q in range(S // 16):
                    sp.dma_start(grouped[:, q * 16 * AW:(q + 1) * 16 * AW], zeros[:, :]).then_inc(cleared, 16)

            @block.vector
            def _(dve):
                dve.memset(one_row[:, :], 1.0)
                dve.memset(pos[:, :], 0.0)
                dve.reduce_sum(total[:, :], mask[:, :, 0:NT].rearrange("p j n -> p n j"), AX.X)\
                   .then_inc(s_tot, 1)
                dve.wait_ge(s_pre, 1)
                dve.tensor_scalar(steps_i[:, :], pp[:, NT:2 * NT], float(P - 1), None, ALU.add)
                dve.tensor_scalar(col_i[0:NT, :], pp[0:NT, 64:65], float(P - 1), None, ALU.add)
                dve.drain()
                dve.tensor_scalar(steps_i[:, :], steps_i[:, :], 7, None, ALU.logical_shift_right)
                dve.tensor_scalar(col_i[0:NT, :], col_i[0:NT, :], 7, None, ALU.logical_shift_right)
                dve.drain()
                dve.tensor_copy(steps_f[:, :], steps_i[:, :])
                dve.tensor_copy(col_f[0:NT, 0:1], col_i[0:NT, :]).then_inc(s_nst, 1)
                dve.drain()
                dve.tensor_tensor_scan(ends[:, :], one_row[:, 0:NT], steps_f[:, :], 0.0, ALU.mult, ALU.add)
                dve.drain()
                dve.tensor_tensor(ends[:, :], ends[:, :], steps_f[:, :], ALU.subtract)
                dve.drain()
                dve.scalar_tensor_tensor(out=offset[:, :], in0=ends[:, :], scalar=float(P), in1=pp[:, 0:NT],
                                         op0=ALU.mult, op1=ALU.add)
                dve.wait_ge(s_end, 1)
                dve.tensor_copy(col_f[0:NT, 1:2], pq[0:NT, 0:1])
                dve.drain()
                dve.tensor_scalar(offset[:, :], offset[:, :], -1.0, None, ALU.add)
                dve.tensor_scalar(passed[0:NT, :], step_no[0:NT, :], col_f[0:NT, 1:2], None, ALU.is_ge)\
                   .then_inc(s_bst, 1)
                with dve.Fori(0, NT) as n:
                    dve.drain()
                    dve.tensor_tensor_scan(rank[:, :], one_row[:, :], mask[:, :, n], 0.0, ALU.mult, ALU.add)
                    dve.drain()
                    dve.scalar_tensor_tensor(out=rank[:, :], in0=rank[:, :], scalar=offset[:, bass.ds(n, 1)],
                                             in1=mask[:, :, n], op0=ALU.add, op1=ALU.mult)
                    dve.drain()
                    dve.tensor_tensor(pos[:, :], pos[:, :], rank[:, :], ALU.add)
                dve.drain()
                dve.tensor_copy(attr_pos[:, :], pos[:, :])
                dve.drain()
                dve.tensor_scalar(place_i[:, 0, :], attr_pos[:, :], P - 1, None, ALU.bitwise_and)
                dve.tensor_scalar(place_i[:, 1, :], attr_pos[:, :], 7, None, ALU.logical_shift_right)
                dve.drain()
                dve.tensor_copy(pos[:, :], place_i[:, 1, :])
                dve.drain()
                dve.scalar_tensor_tensor(out=attr_pos[:, :], in0=place_i[:, 0, :], scalar=float(S),
                                         in1=pos[:, :], op0=ALU.mult, op1=ALU.add)
                dve.wait_ge(s_arow, 1)
                dve.tensor_copy(tileA[:, :], px[:, 0:S])

            @block.tensor
            def _(pe):
                pe.wait_ge(s_tot, 1)
                pe.matmul(pp[:, 0:NT], before[:, :], total[:, :], start=True, stop=True)
                pe.matmul(pp[:, NT:2 * NT], ones[:, :], total[:, :], start=True, stop=True)
                pe.matmul(pp[0:NT, 64:65], total[:, :], ones[:, 0:1], start=True, stop=True)\
                  .then_inc(s_pre, 1)
                pe.wait_ge(s_nst, 1)
                pe.matmul(pq[0:NT, 0:1], upto[0:NT, 0:NT], col_f[0:NT, 0:1], start=True, stop=True)\
                  .then_inc(s_end, 1)
                pe.wait_ge(s_bst, 1)
                pe.matmul(px[:, 0:S], ones[0:NT - 1, :], passed[0:NT - 1, :], start=True, stop=True)\
                  .then_inc(s_arow, 1)

    el_er = sb("el_er", [P, 2, NT, HEADS], scope=edges)
    slot_free, scattered = Signal(lasting_sem("slot_free")), [Signal(lasting_sem(f"scattered{k}")) for k in range(14)]
    staged = [Signal(lasting_sem(f"staged{h}")) for h in range(2)]
    described = Signal(lasting_sem("described"))

    def gat_project(tag, w, al, ar):
        s_w, s_p, s_c = sem(tag + "_w"), sem(tag + "_p"), sem(tag + "_c")
        s_dot = sem(tag + "_dot")
        stored = [sem(f"{tag}_st{k}") for k in range(5)]
        with ExitStack() as scope:
            HT = sb(tag + "_HT", [P, KD, NP], scope=scope)
            to_feature_major(tag + "_t", HB, HT, KD)
            W = sb(tag + "_W", [P, KD, D], scope=scope)
            aa = sb(tag + "_aa", [P, 2, D], scope=scope)
            prod = sb(tag + "_prod", [P, 2, D], scope=scope)
            stage = sb(tag + "_stage", [P, 5, D], scope=scope)
            pf = [psum(f"{tag}_pf{k}", [P, 512], scope=scope) for k in range(5)]
            with nc.Block() as block:
                @block.sync
                def _(sp):
                    sp.dma_start(W[:, :, :], w.rearrange("(c p) m -> p c m", p=P)).then_inc(s_w, 16)
                    for q, a in enumerate((al, ar)):
                        sp.dma_start(aa[:, q, :], a.rearrange("h d -> (h d)").unsqueeze(0)
                                     .to_broadcast([P, D])).then_inc(s_w, 16)
                    rows = feat_d.rearrange("(n p) f -> n p f", p=P)
                    with sp.Fori(0, 5) as i:
                        for k in range(5):
                            sp.wait_ge(s_c, 5 * i + (k + 6))
                            sp.dma_start(rows[5 * i + k, :, :], stage[:, k, :]).then_inc(stored[k], 16)
                    for k in range(5):
                        sp.wait_ge(stored[k], 16 * 5)

                @block.tensor
                def _(pe):
                    pe.sem_inc(s_c, 5)
                    pe.wait_ge(s_w, 48)
                    for i in range(5):
                        for k in range(5):
                            pe.wait_ge(s_c, 5 * i + (k + 1))
                            for c in range(KD):
                                last = pe.matmul(pf[k][:, 0:D], HT[:, c, bass.ds((5 * i + k) * P, P)],
                                                 W[:, c, :], start=(c == 0), stop=(c == KD - 1))
                            last.then_inc(s_p, 1)

                @block.scalar
                def _(act):
                    def turn(i, first=False):
                        for k in range(5):
                            act.wait_ge(s_p, 5 * i + (k + 1))
                            if not first:
                                act.wait_ge(stored[k], 16 * i)
                            act.wait_ge(s_dot, 5 * i + (k + 1))
                            act.copy(stage[:, k, :], pf[k][:, 0:D]).then_inc(s_c, 1)

                    turn(0, first=True)
                    with act.Fori(1, 5) as i:
                        turn(i)

                @block.vector
                def _(dve):
                    dve.wait_ge(s_w, 48)
                    dve.sem_inc(s_dot, 5)
                    with dve.Fori(0, 5) as i:
                        for k in range(5):
                            dve.wait_ge(s_c, 5 * i + (k + 6))
                            for q in range(2):
                                dve.tensor_tensor(prod[:, q, :], stage[:, k, :], aa[:, q, :], ALU.mult)
                            dve.drain()
                            for q in range(2):
                                last = dve.reduce_sum(el_er[:, q, 5 * i + k, :],
                                                      prod[:, q, :].rearrange("p (h d) -> p h d", h=HEADS),
                                                      AX.X)
                            last.then_inc(s_dot, 1)
                            dve.wait_ge(s_dot, 5 * i + (k + 1 + 5))

    def gat_weights(tag, first_turn):
        CH = EC // 4
        s_tab, s_took = sem(tag + "_table"), sem(tag + "_took")
        lo_ready = [sem(f"{tag}_lo{k}") for k in range(7)]
        s_hot, s_look, s_pick, s_sum = (sem(tag + x) for x in ("_hot", "_look", "_pick", "_sum"))
        s_e, s_l1, s_l2, s_tr, s_ex, s_exw, s_rows, s_xt, s_xc = (
            sem(tag + x) for x in ("_e", "_l1", "_l2", "_tr", "_ex", "_exw", "_rows", "_xt", "_xc"))
        sc0 = [c.at for c in scattered]
        st0, de0 = [c.at for c in staged], described.at
        with ExitStack() as scope:
            e = sb(tag + "_e", [P, EC, HEADS], scope=scope)
            m = sb(tag + "_m", [P, EC, HEADS], scope=scope)
            tab = sb(tag + "_tab", [P, 3, 2 * NT * HEADS], BF16, scope)
            rest = sb(tag + "_rest", [P, 2 * NT * HEADS], scope=scope)
            inner = ExitStack()
            lo = sb(tag + "_lo", [P, 7, 2, 4 * P], BF16, inner)
            hot = sb(tag + "_hotT", [P, 2, 2, 4 * P], BF16, inner)
            cand = sb(tag + "_cand", [P, 2, 4, 2 * NT * HEADS], scope=inner)
            abuf = sb(tag + "_abuf", [P, 14, AW], scope=inner)
            aslot = sb(tag + "_aslot", [P, 14], I32, inner)
            pk = [psum(f"{tag}_pk{a}", [P, 2, 512], scope=inner) for a in range(2)]
            block = inner.enter_context(nc.Block())
            attr_v = t["attr"].rearrange("(p j) f -> p j f", p=P)

            @block.sync
            def _(sp):
                with sp.Fori(0, 7) as i:
                    for k in range(14):
                        c = 14 * i + k
                        sp.wait_ge(s_hot, c + 1)
                        for q in range(2):
                            sp.dma_start(lo[:, k % 7, q, :],
                                         lo_d[q, bass.ds(4 * c, 4), :].rearrange("j p -> (j p)")
                                         .unsqueeze(0).to_broadcast([P, 4 * P]))\
                              .then_inc(lo_ready[k % 7], 16)

            @block.scalar
            def _(act):
                def turn(i, first=False):
                    for h in range(2):
                        j0 = 14 * i + (14 * first_turn + 7 * h)
                        for k in range(7 * h, 7 * h + 7):
                            if not first:
                                act.wait_ge(scattered[k].sem, 16 * i + sc0[k])
                        act.dma_start(abuf[:, 7 * h:7 * h + 7, 0:AD], attr_v[:, bass.ds(j0, 7), :])\
                           .then_inc(staged[h].sem, 16)
                        act.copy(abuf[:, 7 * h:7 * h + 7, AD + 1], src_lo[:, bass.ds(j0, 7)])
                        act.copy(aslot[:, 7 * h:7 * h + 7], attr_pos[:, bass.ds(j0, 7)])\
                           .then_inc(described.sem, 1)

                turn(0, first=True)
                with act.Fori(1, 14) as i:
                    turn(i)

            @block.gpsimd
            def _(pool):
                pool.memset(abuf[:, :, AD], 1.0)
                pool.drain()
                pool.wait_ge(cleared, 16 * (S // 16))
                with pool.Fori(0, 14) as i:
                    for h in range(2):
                        pool.wait_ge(staged[h].sem, 16 * i + (st0[h] + 16))
                        pool.wait_ge(described.sem, 2 * i + (de0 + h + 1))
                        pool.sem_inc(s_took, 1)
                        for k in range(7 * h, 7 * h + 7):
                            pool.indirect_dma_start(
                                out=attr_d, in_=abuf[:, k, :], in_offset=None,
                                out_offset=bass.IndirectOffsetOnAxis(ap=aslot[:, k:k + 1], axis=0),
                            ).then_inc(scattered[k].sem, 16)
                for k in range(14):
                    pool.wait_ge(scattered[k].sem, sc0[k] + 16 * 14)

            @block.vector
            def _(dve):
                flat = el_er[:, :, :, :].rearrange("p q n h -> p (q n h)")
                dve.tensor_copy(tab[:, 0, :], flat)
                dve.drain()
                dve.tensor_tensor(rest[:, :], flat, tab[:, 0, :], ALU.subtract)
                dve.drain()
                dve.tensor_copy(tab[:, 1, :], rest[:, :])
                dve.drain()
                dve.tensor_tensor(rest[:, :], rest[:, :], tab[:, 1, :], ALU.subtract)
                dve.drain()
                dve.tensor_copy(tab[:, 2, :], rest[:, :]).then_inc(s_tab, 1)
                dve.sem_inc(s_hot, 7)

                def pick(c, k):
                    dve.wait_ge(s_look, c + 1)
                    if not (isinstance(c, int) and c < 2):
                        dve.wait_ge(s_sum, c - 1)
                    dve.tensor_tensor(
                        cand[:, k % 2, :, :].rearrange("p (b j) (n h) -> p b (j n) h", b=2, h=HEADS),
                        pk[k % 2][:, :, 0:4 * NT * HEADS].rearrange("p b (m h) -> p b m h", h=HEADS),
                        mask[:, bass.ds(4 * c, 4), :].rearrange("p (b j) n -> p b (j n)", b=2).unsqueeze(3)
                        .to_broadcast([P, 2, 4 * NT, HEADS]), ALU.mult).then_inc(s_pick, 1)

                def add_up(c, k):
                    dve.wait_ge(s_pick, c + 3)
                    dve.reduce_sum(e[:, bass.ds(4 * c, 4), :],
                                   cand[:, k % 2, :, :].rearrange("p j (n h) -> p j h n", h=HEADS), AX.X)\
                       .then_inc(s_sum, 1)

                def one_hot(c, i, k):
                    dve.wait_ge(lo_ready[k % 7], 64 * i + 32 * (k // 7 + 1))
                    dve.wait_ge(s_look, c + 1 - 2) if not isinstance(c, int) else (
                        dve.wait_ge(s_look, c - 1) if c >= 2 else None)
                    dve.tensor_scalar(hot[:, k % 2, :, :], lo[:, k % 7, :, :], part[:, 0:1], None,
                                      ALU.is_equal).then_inc(s_hot, 1)

                one_hot(0, 0, 0)
                one_hot(1, 0, 1)
                for k in range(2, 14):
                    pick(k - 2, k - 2)
                    one_hot(k, 0, k)
                    add_up(k - 2, k - 2)
                with dve.Fori(1, 7) as i:
                    for k in range(14):
                        pick(14 * i + (k - 2), k)
                        one_hot(14 * i + k, i, k)
                        add_up(14 * i + (k - 2), k)
                for c in (CH - 2, CH - 1):
                    pick(c, c)
                    add_up(c, c)

            @block.tensor
            def _(pe):
                pe.wait_ge(s_tab, 1)
                pe.sem_inc(s_pick, 2)
                with pe.Fori(0, 7) as i:
                    for k in range(14):
                        c = 14 * i + k
                        pe.wait_ge(s_hot, c + (7 + 1))
                        pe.wait_ge(s_pick, c + 1)
                        for b in range(2):
                            for j in range(2):
                                for q in range(2):
                                    at = (2 * j + q) * NT * HEADS
                                    for part3 in range(3):
                                        last = pe.matmul(
                                            pk[k % 2][:, b, at:at + NT * HEADS],
                                            hot[:, k % 2, q, (2 * b + j) * P:(2 * b + j + 1) * P],
                                            tab[:, part3, q * NT * HEADS:(q + 1) * NT * HEADS],
                                            start=(part3 == 0), stop=(part3 == 2))
                        last.then_inc(s_look, 1)
            inner.close()

            v = sb(tag + "_v", [P, EC, HEADS], scope=scope)
            edge_col = sb(tag + "_edge_col", [P, 2 * HEADS], scope=scope)
            carry = sb(tag + "_carry", [HEADS, 3, P], scope=scope)
            carry_p = sb(tag + "_carry_p", [P, HEADS], scope=scope)
            rows = sb(tag + "_rows", [P, 4, P * HEADS], scope=scope)
            pa = psum(tag + "_pa", [P, 512], scope=scope)
            pb = psum(tag + "_pb", [P, 512], scope=scope)
            px4 = [psum(f"{tag}_px{k}", [P, 512], scope=scope) for k in range(4)]
            NG = [min(P, S - P * g) for g in range(4)]
            with nc.Block() as block:
                @block.vector
                def _(dve):
                    dve.scalar_tensor_tensor(out=e[:, :, :], in0=e[:, :, :], scalar=0.2, in1=e[:, :, :],
                                             op0=ALU.mult, op1=ALU.max)
                    dve.drain()
                    for way, (reset, source, target) in enumerate(((reset_b, e, m), (reset_e, m, v))):
                        rev = slice(None, None, -1) if way else slice(None)
                        end = 0 if way else EC - 1
                        for h in range(HEADS):
                            dve.tensor_tensor_scan(target[:, rev, h], reset[:, rev], source[:, rev, h],
                                                   -BIG, ALU.add, ALU.max)
                        dve.tensor_reduce(edge_col[:, HEADS:HEADS + 1], reset[:, :], AX.X, ALU.min)
                        dve.drain()
                        dve.tensor_copy(edge_col[:, 0:HEADS], target[:, end, :])
                        for h in range(1, HEADS):
                            dve.tensor_copy(edge_col[:, HEADS + h:HEADS + h + 1],
                                            edge_col[:, HEADS:HEADS + 1])
                        dve.drain()
                        dve.sem_inc(s_l1, 1)
                        dve.wait_ge(s_tr, 2 * way + 1)
                        dve.tensor_copy(carry[:, 0, :], pa[0:HEADS, 0:P])
                        dve.tensor_copy(carry[:, 1, :], pa[0:HEADS, P:2 * P])
                        dve.memset(carry[:, 2, :], -BIG)
                        dve.drain()
                        dve.tensor_tensor_scan(carry[:, 0, rev], carry[:, 1, rev], carry[:, 0, rev],
                                               -BIG, ALU.add, ALU.max)
                        dve.drain()
                        if way:
                            dve.tensor_copy(carry[:, 2, 0:P - 1], carry[:, 0, 1:P])
                        else:
                            dve.tensor_copy(carry[:, 2, 1:P], carry[:, 0, 0:P - 1])
                        dve.drain()
                        dve.sem_inc(s_l2, 1)
                        dve.wait_ge(s_tr, 2 * way + 2)
                        dve.tensor_copy(carry_p[:, :], pb[:, 0:HEADS])
                        dve.drain()
                        for h in range(HEADS):
                            dve.tensor_tensor_scan(target[:, rev, h], reset[:, rev], source[:, rev, h],
                                                   carry_p[:, h:h + 1], ALU.add, ALU.max)
                        dve.drain()
                    dve.tensor_tensor(e[:, :, :], e[:, :, :], v[:, :, :], ALU.subtract).then_inc(s_e, 1)
                    for n in range(16):
                        g, h = n // HEADS, n % HEADS
                        dve.wait_ge(s_xt, n + 1)
                        dve.tensor_copy(exS[:, g * P:g * P + NG[g], h], px4[n % 4][:, 0:NG[g]])\
                           .then_inc(s_xc, 1)

                @block.scalar
                def _(act):
                    act.wait_ge(s_e, 1)
                    act.activation(e[:, :, :], e[:, :, :], ACT.Exp).then_inc(s_ex, 1)
                    act.wait_ge(s_ex, 1)
                    act.dma_start(weight_d.rearrange("e (q h) -> (e q) h", h=HEADS)
                                  .rearrange("(p j) h -> p (j h)", p=P),
                                  e[:, :, :].rearrange("p j h -> p (j h)")).then_inc(s_exw, 16)

                @block.gpsimd
                def _(pool):
                    pool.wait_ge(s_exw, 16)
                    for g in range(4):
                        pool.indirect_dma_start(
                            out=rows[0:NG[g], g, :], out_offset=None, in_=weight_d,
                            in_offset=bass.IndirectOffsetOnAxis(ap=edge_tile_k[0:NG[g], g:g + 1], axis=0),
                        ).then_inc(s_rows, 16)

                @block.tensor
                def _(pe):
                    for way in range(2):
                        pe.wait_ge(s_l1, way + 1)
                        pe.transpose(pa[0:HEADS, 0:P], edge_col[:, 0:HEADS], ident[:, :])
                        pe.transpose(pa[0:HEADS, P:2 * P], edge_col[:, HEADS:2 * HEADS], ident[:, :])\
                          .then_inc(s_tr, 1)
                        pe.wait_ge(s_l2, way + 1)
                        pe.transpose(pb[:, 0:HEADS], carry[:, 2, :], ident[0:HEADS, 0:HEADS])\
                          .then_inc(s_tr, 1)
                    pe.wait_ge(s_rows, 64)
                    for n in range(16):
                        g, h = n // HEADS, n % HEADS
                        if n >= 4:
                            pe.wait_ge(s_xc, n - 3)
                        pe.transpose(px4[n % 4][:, 0:NG[g]],
                                     rows[0:NG[g], g, :].rearrange("s (q h) -> s q h", h=HEADS)[:, :, h],
                                     ident[0:NG[g], 0:NG[g]]).then_inc(s_xt, 1)
        for c in scattered:
            c.at += 16 * 14
        for c in staged:
            c.at += 16 * 14
        described.at += 28

    def gat_finish(tag, acc, residual):
        s_sum, s_neg, s_exp = sem(tag + "_sum"), sem(tag + "_neg"), sem(tag + "_exp")
        CT = 5
        with ExitStack() as scope:
            den = sb(tag + "_den", [P, NT, HEADS], scope=scope)
            neg = sb(tag + "_negs", [P, NT, D], scope=scope)
            with nc.Block() as block:
                @block.vector
                def _(dve):
                    if not residual:
                        dve.tensor_copy(in_deg[:, :], acc[:, :, W_GAT - 1])
                    dve.tensor_scalar(den[:, :, :], acc[:, :, D:D + HEADS], 0.5, None, ALU.max)
                    dve.drain()
                    dve.reciprocal(den[:, :, :], den[:, :, :])
                    dve.drain()
                    for c in range(NT // CT):
                        r = slice(CT * c, CT * c + CT)
                        rows = acc[:, r, 0:D].rearrange("p n (h d) -> p n h d", h=HEADS)
                        last = dve.tensor_tensor(rows, rows, den[:, r, :].unsqueeze(3)
                                                 .to_broadcast([P, CT, HEADS, HD]), ALU.mult)
                        if residual:
                            dve.drain()
                            last = dve.tensor_tensor(acc[:, r, 0:D], acc[:, r, 0:D], HB[:, r, :], ALU.add)
                        last.then_inc(s_sum, 1)
                    for c in range(NT // CT):
                        r = slice(CT * c, CT * c + CT)
                        dve.wait_ge(s_exp, c + 1)
                        goal = acc[:, r, 0:D] if residual else HB[:, r, :]
                        dve.scalar_tensor_tensor(out=goal, in0=neg[:, r, :], scalar=-1.0, in1=acc[:, r, 0:D],
                                                 op0=ALU.add, op1=ALU.max)
                    if residual:
                        dve.drain()
                        dve.tensor_tensor(X[:, :, :], X[:, :, :], acc[:, :, 0:D], ALU.add)

                @block.scalar
                def _(act):
                    for c in range(NT // CT):
                        r = slice(CT * c, CT * c + CT)
                        act.wait_ge(s_sum, c + 1)
                        act.activation(neg[:, r, :], acc[:, r, 0:D], ACT.Relu, scale=-1.0).then_inc(s_neg, 1)
                        act.wait_ge(s_neg, c + 1)
                        act.activation(neg[:, r, :], neg[:, r, :], ACT.Exp, scale=-1.0).then_inc(s_exp, 1)

    edge_tile_k = sb("edge_tile_k", [P, 4], I32, edges)
    s_et = sem("edge_tile_again")
    with ExitStack() as scope:
        turned = psum("turned_tiles", [P, 512], scope=scope)
        tile_f2 = sb("tile_f2", [1, S], scope=scope)
        with nc.Block() as block:
            @block.vector
            def _(dve):
                dve.tensor_tensor(tile_f2[:, :], step_no[0:1, :], tileS[0:1, :], ALU.subtract)
                dve.drain()
                dve.sem_inc(s_et, 1)
                dve.wait_ge(s_et, 2)
                for g in range(4):
                    ng = min(P, S - P * g)
                    dve.tensor_copy(edge_tile_k[0:ng, g:g + 1], turned[0:ng, g:g + 1])

            @block.tensor
            def _(pe):
                pe.wait_ge(s_et, 1)
                for g in range(4):
                    ng = min(P, S - P * g)
                    last = pe.matmul(turned[0:ng, g:g + 1], tile_f2[:, g * P:g * P + ng], ones[0:1, 0:1],
                                     start=True, stop=True)
                last.then_inc(s_et, 1)

    end_phase()
    layer_norm("ln0")
    end_phase()
    gat_project("gp1", t["L0_gnn_W1"], t["L0_gnn_al1"], t["L0_gnn_ar1"])
    end_phase()
    gat_weights("gw1", 0)
    end_phase()
    with ExitStack() as scope:
        acc = sb("acc_g1", [P, NT, ACCW], scope=scope)
        aggregate("ga1", feat_d, srcS, acc, "gat")
        end_phase()
        gat_finish("gf1", acc, False)
        end_phase()
    gat_project("gp2", t["L0_gnn_W2"], t["L0_gnn_al2"], t["L0_gnn_ar2"])
    end_phase()
    gat_weights("gw2", 14)
    end_phase()
    edges.close()
    with ExitStack() as scope:
        acc = sb("acc_g2", [P, NT, ACCW], scope=scope)
        aggregate("ga2", feat_d, srcS, acc, "gat")
        end_phase()
        gat_finish("gf2", acc, True)
        end_phase()

    layer_norm("ln1")
    end_phase()
    with ExitStack() as scope:
        acc = sb("acc_a", [P, NT, AW], scope=scope)
        odd = sb("acc_odd", [P, NT, AW], scope=scope)
        aggregate("aga", None, None, acc, "attr", odd)
        end_phase()
        s_w1, s_dg, s_zx, s_zr = sem("l1_w"), sem("l1_deg"), sem("l1_index"), [sem(f"l1_z{k}") for k in range(5)]
        s_zt, s_mm, s_sig, s_free = sem("l1_took"), sem("l1_mm"), sem("l1_sig"), sem("l1_free")
        AT = sb("AT", [P, 1, NP], scope=scope)
        to_feature_major("att", acc, AT, 1)
        wsum = sb("wsum", [P, D], scope=scope)
        bsum = sb("bsum", [P, D], scope=scope)
        enc_l = sb("enc_l", [2, 2, NP], scope=scope)
        enc_r = sb("enc_r", [2, 2, D], scope=scope)
        zi = sb("zi", [P, 2, 5, D], scope=scope)
        deg_f = sb("deg_f", [P, 2, NT], scope=scope)
        deg_i = sb("deg_i", [P, 2, NT], I32, scope)
        zslot = sb("zslot", [P, 2, 5], I32, scope)
        sig = sb("sig", [P, 5, 2, D], scope=scope)
        tmp = sb("l1_tmp", [P, 2, D], scope=scope)
        banks = psum("l1_banks", [P, 8, 512], scope=scope)
        enc_ps = [banks[:, k % 4, :] for k in range(5)]
        sum_ps = [banks[:, 4 + k % 4, 0:D] for k in range(5)]
        with nc.Block() as block:
            @block.sync
            def _(sp):
                sp.dma_start(wsum[:, :], t["L1_gnn_W_sum"]).then_inc(s_w1, 16)
                sp.dma_start(bsum[:, :], t["L1_gnn_b_sum"].unsqueeze(0).to_broadcast([P, D])).then_inc(s_w1, 16)
                for q, (v, w, b) in enumerate((("cent", "L1_gnn_W_cent", "L1_gnn_b_cent"),
                                               ("vor", "L1_gnn_W_vor", "L1_gnn_b_vor"))):
                    sp.dma_start(enc_l[0:1, q, :], t[v].unsqueeze(0)).then_inc(s_w1, 16)
                    sp.dma_start(enc_l[1:2, q, :], t["ones"].unsqueeze(0)).then_inc(s_w1, 16)
                    sp.dma_start(enc_r[0:1, q, :], t[w]).then_inc(s_w1, 16)
                    sp.dma_start(enc_r[1:2, q, :], t[b].unsqueeze(0)).then_inc(s_w1, 16)

            @block.gpsimd
            def _(pool):
                with pool.Fori(0, 5) as i:
                    pool.wait_ge(s_zx, i + 1)
                    pool.sem_inc(s_zt, 1)
                    for k in range(5):
                        for q, table in enumerate(("L1_gnn_z_in", "L1_gnn_z_out")):
                            pool.indirect_dma_start(
                                out=zi[:, q, k, :], out_offset=None, in_=t[table],
                                in_offset=bass.IndirectOffsetOnAxis(ap=zslot[:, q, k:k + 1], axis=0),
                            ).then_inc(s_zr[k], 16)

            @block.scalar
            def _(act):
                act.wait_ge(s_dg, 1)
                with act.Fori(0, 5) as i:
                    act.wait_ge(s_free, 5 * i + 5)
                    act.copy(zslot[:, :, :], deg_i[:, :, bass.ds(5 * i, 5)]).then_inc(s_zx, 1)
                    for k in range(5):
                        act.wait_ge(s_mm, 5 * i + (k + 1))
                        act.activation(sig[:, k, :, :], enc_ps[k].rearrange("p (q f) -> p q f", q=2),
                                       ACT.Sigmoid).then_inc(s_sig, 1)

            @block.tensor
            def _(pe):
                pe.wait_ge(s_w1, 160)
                pe.sem_inc(s_free, 5)
                for i in range(5):
                    for k in range(5):
                        cols = bass.ds((5 * i + k) * P, P)
                        pe.wait_ge(s_free, 5 * i + {0: 5, 4: 6}.get(k, k + 1))
                        for q in range(2):
                            pe.matmul(enc_ps[k][:, q * D:(q + 1) * D], enc_l[:, q, cols], enc_r[:, q, :],
                                      start=True, stop=True)
                        pe.matmul(sum_ps[k], AT[:, 0, cols], wsum[:, :], start=True, stop=True)\
                          .then_inc(s_mm, 1)

            @block.vector
            def _(dve):
                dve.tensor_scalar(deg_f[:, 0, :], in_deg[:, :], 511.0, None, ALU.min)
                dve.tensor_scalar(deg_f[:, 1, :], acc[:, :, AD], 511.0, None, ALU.min)
                dve.drain()
                dve.tensor_copy(deg_i[:, :, :], deg_f[:, :, :]).then_inc(s_dg, 1)
                dve.tensor_tensor(X[:, :, :], X[:, :, :], HB[:, :, :], ALU.add)
                dve.wait_ge(s_w1, 160)
                with dve.Fori(0, 5) as i:
                    for k in range(5):
                        n = 5 * i + k
                        dve.drain()
                        dve.wait_ge(s_mm, n + 1)
                        dve.scalar_tensor_tensor(out=tmp[:, 0, :], in0=bsum[:, :],
                                                 scalar=acc[:, n, AD:AD + 1], in1=sum_ps[k],
                                                 op0=ALU.mult, op1=ALU.add)
                        dve.wait_ge(s_zr[k], 32 * i + 32)
                        dve.tensor_tensor(tmp[:, 1, :], zi[:, 0, k, :], zi[:, 1, k, :], ALU.add)
                        dve.drain()
                        dve.tensor_tensor(tmp[:, 0, :], tmp[:, 0, :], tmp[:, 1, :], ALU.add)
                        dve.drain()
                        dve.wait_ge(s_sig, n + 1)
                        dve.tensor_tensor(tmp[:, 1, :], sig[:, k, 0, :], sig[:, k, 1, :], ALU.add)
                        dve.tensor_tensor(X[:, n, :], X[:, n, :], tmp[:, 0, :], ALU.add)
                        dve.drain()
                        dve.tensor_tensor(X[:, n, :], X[:, n, :], tmp[:, 1, :], ALU.add).then_inc(s_free, 1)

    layer_norm("ln2")
    end_phase()
    s_wz, s_wb, s_r = sem("rel_zero"), sem("rel_w"), [sem(f"rel_mm{q}") for q in range(2)]
    s_re = [sem(f"rel_copy{q}") for q in range(2)]
    s_rst = [sem(f"rel_stored{k}") for k in range(5)]
    with ExitStack() as scope:
        HT = sb("HT2", [P, KD, NP], scope=scope)
        to_feature_major("t2", HB, HT, KD)
        blocks = sb("blocks", [P, KD, RELS, P], scope=scope)
        stage = sb("rel_stage", [P, 5, RELS, D], scope=scope)
        SUB = D // 8
        banks = [psum(f"rel_ps{k}", [P, 512], scope=scope) for k in range(4)]
        with nc.Block() as block:
            @block.gpsimd
            def _(pool):
                pool.memset(blocks[:, :, :, :], 0.0).then_inc(s_wz, 1)

            @block.sync
            def _(sp):
                sp.wait_ge(s_wz, 1)
                w = t["L2_gnn_weight"].rearrange("r (b i o) -> b i r o", b=8, i=SUB)
                for b in range(8):
                    at = b % 4 * SUB
                    sp.dma_start(blocks[at:at + SUB, b // 4, :, at:at + SUB], w[b]).then_inc(s_wb, 16)
                rows = rel_d.rearrange("(n p r) f -> n p (r f)", p=P, r=RELS)
                with sp.Fori(0, 5) as i:
                    for k in range(5):
                        for q in range(2):
                            sp.wait_ge(s_re[q], 2 * (5 * i + k) + 4)
                        sp.dma_start(rows[5 * i + k, :, :],
                                     stage[:, k, :, :].rearrange("p r f -> p (r f)")).then_inc(s_rst[k], 16)
                for k in range(5):
                    sp.wait_ge(s_rst[k], 80)

            @block.tensor
            def _(pe):
                pe.wait_ge(s_wb, 128)
                for q in range(2):
                    pe.sem_inc(s_re[q], 2)
                for n in range(NT):
                    for c in range(KD):
                        for g in range(2):
                            pe.wait_ge(s_re[g], 2 * n + (c + 1))
                            pe.matmul(banks[2 * c + g][:, :], HT[:, c, bass.ds(n * P, P)],
                                      blocks[:, c, 4 * g:4 * g + 4, :], start=True, stop=True)\
                              .then_inc(s_r[g], 1)

            def copy_relations(eng, g, copy):
                def turn(i, first=False):
                    for k in range(5):
                        if not first:
                            eng.wait_ge(s_rst[k], 16 * i)
                        for c in range(KD):
                            eng.wait_ge(s_r[g], 2 * (5 * i + k) + (c + 1))
                            copy(stage[:, k, 4 * g:4 * g + 4, c * P:(c + 1) * P],
                                 banks[2 * c + g][:, :].rearrange("p (r o) -> p r o", r=4))\
                                .then_inc(s_re[g], 1)

                turn(0, first=True)
                with eng.Fori(1, 5) as i:
                    turn(i)

            @block.scalar
            def _(act):
                copy_relations(act, 0, act.copy)

            @block.vector
            def _(dve):
                copy_relations(dve, 1, dve.tensor_copy)

    with ExitStack() as scope:
        acc = sb("acc_r", [P, NT, D], scope=scope)
        aggregate("agr", rel_d, relS, acc, "edge")
        end_phase()
        with nc.Block() as block:
            @block.vector
            def _(dve):
                dve.tensor_tensor(X[:, :, :], X[:, :, :], acc[:, :, :], ALU.add)

    layer_norm("ln3")
    end_phase()
    G = sb("G", [P, KD, NP])
    bn = sb("bn", [P, KD, 8, 6])
    bmv = sb("bmv", [P, KD, 2])
    bsc = sb("bsc", [P, KD, 2])
    RUNS = [(at, min(512, N - at)) for at in range(0, N, 512)]
    to_feature_major("t3", HB, G, KD)

    def conv_project(tag, w, b):
        s_w, s_p, s_c, s_r = sem(tag + "_w"), sem(tag + "_p"), sem(tag + "_c"), sem(tag + "_r")
        stored = [sem(f"{tag}_st{k}") for k in range(5)]
        with ExitStack() as scope:
            W = sb(tag + "_W", [P, KD, D], scope=scope)
            bias = sb(tag + "_bias", [P, D], scope=scope)
            stage = sb(tag + "_stage", [P, 5, D], scope=scope)
            pf = [psum(f"{tag}_pf{k}", [P, 512], scope=scope) for k in range(5)]
            with nc.Block() as block:
                @block.sync
                def _(sp):
                    sp.dma_start(W[:, :, :], w.rearrange("(c p) m -> p c m", p=P)).then_inc(s_w, 16)
                    sp.dma_start(bias[:, :], b.unsqueeze(0).to_broadcast([P, D])).then_inc(s_w, 16)
                    rows = feat_d.rearrange("(n p) f -> n p f", p=P)
                    with sp.Fori(0, 5) as i:
                        for k in range(5):
                            sp.wait_ge(s_r, 5 * i + (k + 1))
                            sp.dma_start(rows[5 * i + k, :, :], stage[:, k, :]).then_inc(stored[k], 16)
                    for k in range(5):
                        sp.wait_ge(stored[k], 16 * 5)

                @block.tensor
                def _(pe):
                    pe.sem_inc(s_c, 5)
                    pe.wait_ge(s_w, 32)
                    for i in range(5):
                        for k in range(5):
                            pe.wait_ge(s_c, 5 * i + (k + 1))
                            for c in range(KD):
                                last = pe.matmul(pf[k][:, 0:D], G[:, c, bass.ds((5 * i + k) * P, P)],
                                                 W[:, c, :], start=(c == 0), stop=(c == KD - 1))
                            last.then_inc(s_p, 1)

                @block.scalar
                def _(act):
                    with act.Fori(0, 5) as i:
                        for k in range(5):
                            act.wait_ge(s_c, 5 * i + (k + 6))
                            act.activation(stage[:, k, :], stage[:, k, :], ACT.Relu).then_inc(s_r, 1)

                @block.vector
                def _(dve):
                    dve.wait_ge(s_w, 32)

                    def turn(i, first=False):
                        for k in range(5):
                            dve.wait_ge(s_p, 5 * i + (k + 1))
                            if not first:
                                dve.wait_ge(stored[k], 16 * i)
                            dve.tensor_tensor(stage[:, k, :], pf[k][:, 0:D], bias[:, :], ALU.add)\
                               .then_inc(s_c, 1)

                    turn(0, first=True)
                    with dve.Fori(1, 5) as i:
                        turn(i)

    def conv_finish(tag, acc, w, b, norms):
        s_w, s_p, s_c = sem(tag + "_w"), sem(tag + "_p"), sem(tag + "_c")
        s_n, s_a = sem(tag + "_norm"), sem(tag + "_applied")
        NC = 8
        CN = NP // NC
        with ExitStack() as scope:
            AT = sb(tag + "_AT", [P, KD, NP], scope=scope)
            to_feature_major(tag + "_t", acc, AT, KD)
            W = sb(tag + "_W", [P, KD, D], scope=scope)
            bias = sb(tag + "_bias", [P, KD], scope=scope)
            gb = sb(tag + "_gb", [P, len(norms), 2, KD], scope=scope)
            pf = [psum(f"{tag}_pf{k}", [P, 512], scope=scope) for k in range(4)]
            n_load = 16 * (2 + 2 * len(norms))
            with nc.Block() as block:
                @block.sync
                def _(sp):
                    sp.dma_start(W[:, :, :], w.rearrange("(c p) m -> p c m", p=P)).then_inc(s_w, 16)
                    sp.dma_start(bias[:, :], b.rearrange("(c p) -> p c", p=P),
                                 allow_slow_non_contiguous=True).then_inc(s_w, 16)
                    for z, (gamma, beta, _) in enumerate(norms):
                        for q, v in enumerate((gamma, beta)):
                            sp.dma_start(gb[:, z, q, :], v.rearrange("(c p) -> p c", p=P),
                                         allow_slow_non_contiguous=True).then_inc(s_w, 16)

                @block.tensor
                def _(pe):
                    pe.wait_ge(s_w, n_load)
                    for u in range(NC * KD):
                        r, c = u // KD, u % KD
                        if u >= 4:
                            pe.wait_ge(s_c, u - 3)
                        for a in range(KD):
                            last = pe.matmul(pf[u % 4][:, 0:CN], W[:, a, c * P:(c + 1) * P],
                                             AT[:, a, r * CN:(r + 1) * CN], start=(a == 0), stop=(a == KD - 1))
                        last.then_inc(s_p, 1)

                @block.scalar
                def _(act):
                    act.wait_ge(s_w, n_load)
                    for u in range(NC * KD):
                        r, c = u // KD, u % KD
                        act.wait_ge(s_p, u + 1)
                        act.activation(G[:, c, r * CN:(r + 1) * CN], pf[u % 4][:, 0:CN], ACT.Identity,
                                       bias=bias[:, c:c + 1]).then_inc(s_c, 1)
                    for z, (_, _, relu) in enumerate(norms):
                        act.wait_ge(s_n, 2 * z + 1)
                        act.activation(bsc[:, :, 0], bsc[:, :, 0], ACT.Sqrt).then_inc(s_a, 1)
                        act.wait_ge(s_n, 2 * z + 2)
                        for c in range(KD):
                            last = act.activation(G[:, c, :], G[:, c, :], ACT.Relu if relu else ACT.Identity,
                                                  bias=bsc[:, c, 1:2], scale=bsc[:, c, 0:1])
                        last.then_inc(s_a, 1)

                @block.vector
                def _(dve):
                    dve.wait_ge(s_w, n_load)
                    dve.wait_ge(s_c, NC * KD)
                    for z in range(len(norms)):
                        if z:
                            dve.wait_ge(s_a, 2 * z)
                        for c in range(KD):
                            for r, (at, size) in enumerate(RUNS):
                                dve.bn_stats(bn[:, c, r, :], G[:, c, at:at + size])
                        dve.drain()
                        for c in range(KD):
                            dve.bn_aggr(bmv[:, c, :], bn[:, c, 0:len(RUNS), :].rearrange("p r s -> p (r s)"))
                        dve.drain()
                        dve.tensor_scalar(bsc[:, :, 0], bmv[:, :, 1], BN_EPS, None, ALU.add).then_inc(s_n, 1)
                        dve.wait_ge(s_a, 2 * z + 1)
                        dve.reciprocal(bsc[:, :, 0], bsc[:, :, 0])
                        dve.drain()
                        dve.tensor_tensor(bsc[:, :, 0], bsc[:, :, 0], gb[:, z, 0, :], ALU.mult)
                        dve.drain()
                        dve.tensor_tensor(bmv[:, :, 0], bmv[:, :, 0], bsc[:, :, 0], ALU.mult)
                        dve.drain()
                        dve.tensor_tensor(bsc[:, :, 1], gb[:, z, 1, :], bmv[:, :, 0], ALU.subtract)\
                           .then_inc(s_n, 1)

    for z, tag in enumerate(("c1", "c2")):
        conv_project(f"{tag}p", t[f"L3_gnn_{tag}_w1"], t[f"L3_gnn_{tag}_b1"])
        end_phase()
        with ExitStack() as scope:
            acc = sb(f"acc_{tag}", [P, NT, D], scope=scope)
            aggregate(f"ag{tag}", feat_d, srcS, acc, "edge")
            end_phase()
            conv_finish(f"{tag}f", acc, t[f"L3_gnn_{tag}_w2"], t[f"L3_gnn_{tag}_b2"],
                        [(t[f"L3_gnn_{tag}_g"], t[f"L3_gnn_{tag}_b"], True),
                         (t[f"L3_gnn_bn{z + 1}_g"], t[f"L3_gnn_bn{z + 1}_b"], z == 0)])
        end_phase()

    s_t, s_x = sem("out_turned"), sem("out_added")
    s_out = [sem(f"out_stored{k}") for k in range(5)]
    with ExitStack() as scope:
        tmp = sb("out_tmp", [P, 5, D], scope=scope)
        pt = [psum(f"out_pt{k}", [P, 512], scope=scope) for k in range(5)]
        with nc.Block() as block:
            @block.tensor
            def _(pe):
                pe.sem_inc(s_x, 5)
                for i in range(5):
                    for k in range(5):
                        pe.wait_ge(s_x, 5 * i + (k + 1))
                        for c in range(KD):
                            last = pe.transpose(pt[k][:, c * P:(c + 1) * P],
                                                G[:, c, bass.ds((5 * i + k) * P, P)], ident[:, :])
                        last.then_inc(s_t, 1)

            @block.vector
            def _(dve):
                with dve.Fori(0, 5) as i:
                    for k in range(5):
                        n = 5 * i + k
                        dve.wait_ge(s_t, n + 1)
                        dve.tensor_tensor(tmp[:, k, :], pt[k][:, 0:D], HB[:, n, :], ALU.add)
                        dve.drain()
                        dve.scalar_tensor_tensor(out=X[:, n, :], in0=tmp[:, k, :], scalar=0.0,
                                                 in1=X[:, n, :], op0=ALU.max, op1=ALU.add).then_inc(s_x, 1)

            @block.sync
            def _(sp):
                rows = out[0:(NT - 1) * P, :].rearrange("(n p) f -> p n f", p=P)
                for k in range(4):
                    sp.wait_ge(s_x, 5 + 6 * k + 6)
                    sp.dma_start(rows[:, 6 * k:6 * k + 6, :], X[:, 6 * k:6 * k + 6, :]).then_inc(s_out[k], 16)
                sp.wait_ge(s_x, 5 + NT)
                sp.dma_start(out[(NT - 1) * P:N, :], X[0:N - (NT - 1) * P, NT - 1, :]).then_inc(s_out[4], 16)
                for k in range(5):
                    sp.wait_ge(s_out[k], 16)
    life.close()


def kernel(**inputs):
    import numpy as np
    import concourse.bacc as bacc
    from concourse.bass_utils import run_bass_kernel_spmd

    a = {k: np.asarray(v) for k, v in inputs.items()}

    def padded(v, rows, fill=0):
        out = np.full((rows,) + v.shape[1:], fill, v.dtype)
        out[:v.shape[0]] = v
        return out

    arrays = {
        "x": padded(a["x"], NP),
        "src": padded(a["src"], EP, PAD_NODE),
        "dst": padded(a["dst"], EP, PAD_NODE),
        "dst_ext": np.full(EP + 2, -1, a["dst"].dtype),
        "type": padded(a["edge_type_8"], EP),
        "weight": padded(a["edge_weight"], EP),
        "attr": padded(a["edge_attr_128"], EP),
        "vor": padded(a["node_vec1"], NP).reshape(NP),
        "cent": padded(a["node_vec1_n2"], NP).reshape(NP),
        "ones": np.ones(NP, np.float32),
    }
    arrays["dst_ext"][1:EP + 1] = arrays["dst"]
    for name in a:
        if name[0] == "L":
            arrays[name] = np.ascontiguousarray(a[name])
    nc = bacc.Bacc("TRN2", target_bir_lowering=False, num_devices=1)
    t = {k: nc.dram_tensor(f"in_{k}", v.shape, mybir.dt.from_np(v.dtype), kind="ExternalInput").ap()
         for k, v in arrays.items()}
    out = nc.dram_tensor("out_0", (N, D), F32, kind="ExternalOutput").ap()
    gnn_program(nc, t, out)
    result = run_bass_kernel_spmd(nc, [{f"in_{k}": v for k, v in arrays.items()}], core_ids=[0])
    return result.results[0]["out_0"]
```
